# Optimizing a Trainium2 kernel written in Bass

```python
import numpy as np
import jax
import jax.numpy as jnp

def _softmax(x, axis=-1):
    return jax.nn.softmax(x, axis=axis)

def _gelu(x):
    return jax.nn.gelu(x, approximate=True)

def _silu(x):
    return jax.nn.silu(x)

def _sigmoid(x):
    return jax.nn.sigmoid(x)

def _layernorm(x, axis=-1, eps=1e-05):
    m = jnp.mean(x, axis=axis, keepdims=True)
    v = jnp.var(x, axis=axis, keepdims=True)
    return (x - m) / jnp.sqrt(v + eps)

def _scatter_add(tgt, idx, src, axis=0):
    return tgt.at[idx].add(src)

def _segment_sum(src, seg, n):
    return jax.ops.segment_sum(src, seg, n)
kernel_name = 'mk_gnn_preln_d2_gnn_r8_9c4614'

def setup_inputs(seed: int=0):
    np.random.seed(seed)
    _w = jnp.asarray

    def _rec_inputs():
        import jax
        import jax.numpy as jnp
        _gk = jax.random.key(seed)
        x = -0.0005121 + 1.001 * jax.random.normal(jax.random.fold_in(_gk, 1), (12500, 64), jnp.float32)
        src = jax.random.randint(jax.random.fold_in(_gk, 2), (200000,), 0, 12500, jnp.int32)
        dst = jnp.minimum((12500 * jax.random.uniform(jax.random.fold_in(_gk, 3), (200000,)) ** 2.0).astype(jnp.int32), 99999)
        _o = jnp.argsort(dst, stable=True)
        src = src[_o]
        dst = dst[_o]
        edge_type_16 = jax.random.randint(jax.random.fold_in(_gk, 13), (200000,), 0, 16, jnp.int32)
        return (x, src, dst, edge_type_16)
    x, src, dst, edge_type_16 = _rec_inputs()

    def _L0_gnn_setup():
        import jax, jax.numpy as jnp
        import numpy as np
        N = 6250
        E = 200000
        D = 64
        NEG_SLOPE = 0.2
        EPS = 1e-16

        def _gat_conv(x, src, dst, W, a_src, a_dst, b, heads, out_ch, concat):
            n = x.shape[0]
            xp = (x @ W).reshape(n, heads, out_ch)
            al_s = jnp.sum(xp * a_src[None], axis=-1)
            al_d = jnp.sum(xp * a_dst[None], axis=-1)
            e = jax.nn.leaky_relu(al_s[src] + al_d[dst], NEG_SLOPE)
            m = jax.ops.segment_max(e, dst, num_segments=n)
            e = jnp.exp(e - m[dst])
            denom = jax.ops.segment_sum(e, dst, num_segments=n)
            alpha = e / (denom[dst] + EPS)
            msg = xp[src] * alpha[:, :, None]
            out = jax.ops.segment_sum(msg, dst, num_segments=n)
            if concat:
                out = out.reshape(n, heads * out_ch)
            else:
                out = out.mean(axis=1)
            return out + b
        key = jax.random.key(seed)
        ks = jax.random.split(key, 16)
        x = jax.random.normal(ks[0], (N, D), dtype=jnp.float32)
        edge_index = jax.random.randint(ks[1], (2, E), 0, N, dtype=jnp.int64)
        s = 0.1
        return {'x': x, 'edge_index': edge_index, 'W1': jax.random.normal(ks[2], (D, 64), dtype=jnp.float32) * s, 'a1_src': jax.random.normal(ks[3], (8, 8), dtype=jnp.float32) * s, 'a1_dst': jax.random.normal(ks[4], (8, 8), dtype=jnp.float32) * s, 'b1': jnp.zeros((64,), dtype=jnp.float32), 'W2': jax.random.normal(ks[5], (64, 64), dtype=jnp.float32) * s, 'a2_src': jax.random.normal(ks[6], (8, 8), dtype=jnp.float32) * s, 'a2_dst': jax.random.normal(ks[7], (8, 8), dtype=jnp.float32) * s, 'b2': jnp.zeros((64,), dtype=jnp.float32), 'W3': jax.random.normal(ks[8], (64, 64), dtype=jnp.float32) * s, 'a3_src': jax.random.normal(ks[9], (1, 64), dtype=jnp.float32) * s, 'a3_dst': jax.random.normal(ks[10], (1, 64), dtype=jnp.float32) * s, 'b3': jnp.zeros((64,), dtype=jnp.float32)}
    _L0_gnn_all = _L0_gnn_setup()
    _L0_gnn_in = {k: v for k, v in _L0_gnn_all.items() if k in ('W1', 'a1_src', 'a1_dst', 'b1', 'W2', 'a2_src', 'a2_dst', 'b2', 'W3', 'a3_src', 'a3_dst', 'b3')}
    del _L0_gnn_all

    def _L1_gnn_setup():
        import jax, jax.numpy as jnp
        import numpy as np
        N_NODES = 6250
        N_EDGES = 100000
        D_IN = 64
        D_OUT = 64
        NUM_RELS = 16
        key = jax.random.key(seed)
        k1, k2, k3, k4, k5 = jax.random.split(key, 5)
        feat = jax.random.normal(k1, (N_NODES, D_IN), dtype=jnp.float32)
        weight = jax.random.normal(k2, (NUM_RELS, D_IN, D_OUT), dtype=jnp.float32) * 0.05
        src = jax.random.randint(k3, (N_EDGES,), 0, N_NODES, dtype=jnp.int32)
        dst = jax.random.randint(k4, (N_EDGES,), 0, N_NODES, dtype=jnp.int32)
        etypes = jax.random.randint(k5, (N_EDGES,), 0, NUM_RELS, dtype=jnp.int32)
        return {'feat': feat, 'weight': weight, 'src': src, 'dst': dst, 'etypes': etypes}
    _L1_gnn_all = _L1_gnn_setup()
    _L1_gnn_in = {k: v for k, v in _L1_gnn_all.items() if k in ('weight',)}
    del _L1_gnn_all
    return {'x': x, 'src': src, 'dst': dst, 'edge_type_16': edge_type_16, 'L0_gnn_W1': _L0_gnn_in['W1'], 'L0_gnn_a1_src': _L0_gnn_in['a1_src'], 'L0_gnn_a1_dst': _L0_gnn_in['a1_dst'], 'L0_gnn_b1': _L0_gnn_in['b1'], 'L0_gnn_W2': _L0_gnn_in['W2'], 'L0_gnn_a2_src': _L0_gnn_in['a2_src'], 'L0_gnn_a2_dst': _L0_gnn_in['a2_dst'], 'L0_gnn_b2': _L0_gnn_in['b2'], 'L0_gnn_W3': _L0_gnn_in['W3'], 'L0_gnn_a3_src': _L0_gnn_in['a3_src'], 'L0_gnn_a3_dst': _L0_gnn_in['a3_dst'], 'L0_gnn_b3': _L0_gnn_in['b3'], 'L1_gnn_weight': _L1_gnn_in['weight']}

def reference(x, src, dst, edge_type_16, L0_gnn_W1, L0_gnn_a1_src, L0_gnn_a1_dst, L0_gnn_b1, L0_gnn_W2, L0_gnn_a2_src, L0_gnn_a2_dst, L0_gnn_b2, L0_gnn_W3, L0_gnn_a3_src, L0_gnn_a3_dst, L0_gnn_b3, L1_gnn_weight):
    import jax
    import jax.numpy as jnp

    def _L0_gnn_ref(x, edge_index, W1, a1_src, a1_dst, b1, W2, a2_src, a2_dst, b2, W3, a3_src, a3_dst, b3):
        import jax, jax.numpy as jnp
        import numpy as np
        N = 6250
        E = 200000
        D = 64
        NEG_SLOPE = 0.2
        EPS = 1e-16

        def _gat_conv(x, src, dst, W, a_src, a_dst, b, heads, out_ch, concat):
            n = x.shape[0]
            xp = (x @ W).reshape(n, heads, out_ch)
            al_s = jnp.sum(xp * a_src[None], axis=-1)
            al_d = jnp.sum(xp * a_dst[None], axis=-1)
            e = jax.nn.leaky_relu(al_s[src] + al_d[dst], NEG_SLOPE)
            m = jax.ops.segment_max(e, dst, num_segments=n)
            e = jnp.exp(e - m[dst])
            denom = jax.ops.segment_sum(e, dst, num_segments=n)
            alpha = e / (denom[dst] + EPS)
            msg = xp[src] * alpha[:, :, None]
            out = jax.ops.segment_sum(msg, dst, num_segments=n)
            if concat:
                out = out.reshape(n, heads * out_ch)
            else:
                out = out.mean(axis=1)
            return out + b
        n = x.shape[0]
        loops = jnp.arange(n, dtype=edge_index.dtype)
        src = jnp.concatenate([edge_index[0], loops])
        dst = jnp.concatenate([edge_index[1], loops])
        x_copy = x
        h = jax.nn.elu(_gat_conv(x, src, dst, W1, a1_src, a1_dst, b1, 8, 8, True))
        h = jax.nn.elu(_gat_conv(h, src, dst, W2, a2_src, a2_dst, b2, 8, 8, True))
        h = _gat_conv(h, src, dst, W3, a3_src, a3_dst, b3, 1, 64, False)
        return h + x_copy

    def _L1_gnn_ref(feat, weight, src, dst, etypes):
        import jax, jax.numpy as jnp
        import numpy as np
        N_NODES = 6250
        N_EDGES = 100000
        D_IN = 64
        D_OUT = 64
        NUM_RELS = 16
        num_rels = weight.shape[0]
        h_src = feat[src]
        msg = jnp.zeros((h_src.shape[0], weight.shape[2]), dtype=feat.dtype)
        for r in range(num_rels):
            mask = etypes == r
            msg = msg + h_src * mask[:, None].astype(feat.dtype) @ weight[r]
        out = jax.ops.segment_sum(msg, dst, num_segments=feat.shape[0])
        return out
    edge_index = jnp.stack([src, dst])
    h = jnp.maximum(_layernorm(x, axis=-1), 0.0)
    x = x + _L0_gnn_ref(h, edge_index, L0_gnn_W1, L0_gnn_a1_src, L0_gnn_a1_dst, L0_gnn_b1, L0_gnn_W2, L0_gnn_a2_src, L0_gnn_a2_dst, L0_gnn_b2, L0_gnn_W3, L0_gnn_a3_src, L0_gnn_a3_dst, L0_gnn_b3)
    h = jnp.maximum(_layernorm(x, axis=-1), 0.0)
    x = x + _L1_gnn_ref(h, L1_gnn_weight, src, dst, edge_type_16)
    return x

_drawn_inputs = setup_inputs


def setup_inputs(seed=0):
    import zlib

    import numpy as np

    out = dict(_drawn_inputs(seed))
    spreads = {'L0_gnn_b1': (0.0, 0.1), 'L0_gnn_b2': (0.0, 0.1), 'L0_gnn_b3': (0.0, 0.1)}
    factors = {'L0_gnn_a1_src': 8.0,
     'L0_gnn_a1_dst': 64.0,
     'L0_gnn_a2_src': 64.0,
     'L0_gnn_a2_dst': 196.084,
     'L0_gnn_a3_src': 64.0,
     'L0_gnn_a3_dst': 200.0}
    for name, (base, spread) in spreads.items():
        noise = np.random.default_rng([zlib.crc32(name.encode()), seed]).standard_normal(out[name].shape)
        drawn = base * np.exp(spread * noise) if base else spread * noise
        out[name] = jnp.asarray(drawn.astype(out[name].dtype))
    for name, factor in factors.items():
        out[name] = (out[name] * factor).astype(out[name].dtype)
    return out
```

```python
from contextlib import ExitStack

import concourse.bass as bass
from concourse import mybir

ALU = mybir.AluOpType
ACT = mybir.ActivationFunctionType
F32 = mybir.dt.float32
BF16 = mybir.dt.bfloat16
I32 = mybir.dt.int32
AX = mybir.AxisListType

P = 128
N, D, H, C = 12500, 64, 8, 8
E, R = 200000, 16
NB = -(-N // P)
NPAD = NB * P
TILES = -(-E // P)
GP = 16
NG = -(-(TILES + NB) // GP)
NP = NG * GP
NC = NP // P
U = 4
XW = 80
TW = 72
DW = 3 * H
SW = 80
CB = 7
NCH = NB // CB
BIG = 1e30
NODST = 30000
LOGMIN = -300.0
assert NB % CB == 0 and NG % U == 0 and NP % P == 0 and NP >= TILES + NB


class Build:

    def __init__(self, nc, ctx):
        self.nc, self.ctx, self.phase_sems = nc, ctx, []

    def sb(self, name, shape, dt=F32):
        return self.ctx.enter_context(self.nc.sbuf_tensor(name, shape, dt))

    def sem(self, name):
        self.phase_sems.append(self.nc.alloc_semaphore(name=name))
        return self.phase_sems[-1]

    def end_phase(self):
        self.nc.clear_and_free_semaphores(self.phase_sems)
        self.phase_sems = []
        self.nc.all_engine_barrier()

    def dram(self, name, shape, dt=F32):
        return self.nc.dram_tensor(name, shape, dt).ap()


def index_phase(nc, top, src, dst, etype, shared):
    ident, iota_row = shared["ident"], shared["iota_row"]
    ones = shared["ones"]
    rows_of = {k: top.dram(f"{k}_rows", (NP, P), I32) for k in ("dst", "src", "rel")}
    row_dram = top.dram("pair_rows", (4, NP), F32)
    given = {"dst": dst, "src": src, "rel": etype}
    whole = (E // P) * P
    rest = E - whole
    with ExitStack() as ctx:
        sb = lambda n, s, d=F32: ctx.enter_context(nc.sbuf_tensor(n, s, d))
        ps = lambda n, s, d=F32: ctx.enter_context(nc.psum_tensor(n, s, d))
        pad = {"dst": sb("pad_dst", [P, P], I32), "src": sb("pad_src", [P, P], I32)}
        pad["rel"] = pad["src"]
        iota_i = sb("iota_i", [P, P], I32)
        tile_no = sb("tile_no", [P, NC], I32)
        pair_no = sb("pair_no", [P, NC], I32)
        tile_nf = sb("tile_nf", [P, NC])
        pair_nf = sb("pair_nf", [P, NC])
        part_i = sb("part_i", [P, 1], I32)
        part_f = shared["part_f"]
        last_i = sb("last_i", [P, NC], I32)
        last_b = sb("last_b", [P, NC], I32)
        last_f = sb("last_f", [P, NC])
        key = sb("key", [P, NC])
        diag = sb("diag", [P, NC, P])
        junk = sb("junk", [P, NP])
        tile_f = sb("tile_f", [P, NC])
        tile_i = sb("tile_i", [P, NC], I32)
        block_f = sb("block_f", [P, NC])
        block0 = sb("block0", [P, NC])
        cnt = sb("cnt", [P, 1])
        pint = sb("pint", [P, P], I32)
        pq = sb("pq", [P, P], I32)
        pqf = sb("pqf", [P, P])
        prf = sb("prf", [P, P])
        got_i = {k: sb(f"got_{k}", [P, NC, P], I32) for k in ("dst", "src", "rel")}
        edge_f = {k: sb(f"edge_{k}", [P, NC, P]) for k in ("dst", "src", "rel", "pf", "la")}
        pen = sb("pen", [P, NC, P + 1])
        ends = sb("ends", [P, 4, NC])
        rows = sb("rows", [1, 3, NP])
        same = sb("same", [1, NP])
        blk = sb("blk", [1, NP])
        idx_e = {k: sb(f"idx_{k}", [P, NP], I32) for k in ("src", "rel")}
        turn = ps("turn", [P, 2, 512])
        wide = ps("wide", [P, 4, 512])
        s_pad = top.sem("pre_padded")
        s_iota = top.sem("pre_iota")
        s_v = top.sem("pre_vector_step")
        s_in = top.sem("pre_rows_in")
        s_last = top.sem("pre_last_in")
        s_wide = top.sem("pre_wide_ready")
        s_gat = top.sem("pre_rows_gathered")
        s_turn = top.sem("pre_turned")
        s_copied = top.sem("pre_copied")
        s_out = top.sem("pre_out")
        s_row = top.sem("pre_row_in")
        s_keys = top.sem("pre_keys")
        s_tiles = top.sem("pre_tiles_known")
        s_ready = top.sem("pre_edge_arrays")
        s_store = top.sem("pre_store")
        s_lp = top.sem("pre_last_pair")
        block = ctx.enter_context(nc.Block())
        order = ("dst", "src", "rel", "pf", "la")

        @block.gpsimd
        def _(pool):
            nc.gpsimd.memset(pad["dst"][:], NODST).then_inc(s_pad, 1)
            nc.gpsimd.memset(pad["src"][:], 0).then_inc(s_pad, 1)
            nc.gpsimd.iota(iota_i[:], pattern=[[1, P]], base=0, channel_multiplier=0).then_inc(s_iota, 1)
            nc.gpsimd.iota(tile_no[:], pattern=[[1, NC]], base=0, channel_multiplier=NC).then_inc(s_iota, 1)
            nc.gpsimd.iota(pair_no[:], pattern=[[P, NC]], base=0, channel_multiplier=1).then_inc(s_iota, 1)
            nc.gpsimd.iota(part_i[:], pattern=[[1, 1]], base=0, channel_multiplier=1).then_inc(s_iota, 1)
            pool.wait_ge(s_tiles, 1)
            for k in ("dst", "src", "rel"):
                for c in range(NC):
                    nc.gpsimd.indirect_dma_start(
                        out=got_i[k][:, c, :], out_offset=None, in_=rows_of[k],
                        in_offset=bass.IndirectOffsetOnAxis(ap=tile_i[:, c:c + 1], axis=0)).then_inc(s_gat, 16)

        @block.sync
        def _(sp):
            sp.wait_ge(s_pad, 2)
            pad_rows = NP - TILES
            for k in ("dst", "src", "rel"):
                flat = rows_of[k].rearrange("t e -> (t e)")
                sp.dma_start(flat[0:whole].rearrange("(a b) -> a b", a=16),
                             given[k][0:whole].rearrange("(a b) -> a b", a=16)).then_inc(s_in, 16)
                sp.dma_start(rows_of[k][TILES - 1:TILES, 0:rest],
                             given[k][whole:E].rearrange("(a b) -> a b", a=1)).then_inc(s_in, 16)
                sp.dma_start(rows_of[k][TILES - 1:TILES, rest:P], pad[k][0:1, rest:P]).then_inc(s_in, 16)
                sp.dma_start(rows_of[k][TILES:NP, :], pad[k][0:pad_rows, :]).then_inc(s_in, 16)
            sp.wait_ge(s_in, 16 * 12)
            sp.dma_start(last_i[:], rows_of["dst"].rearrange("(q c) e -> q c e", c=NC)[:, :, P - 1],
                         allow_slow_non_contiguous=True).then_inc(s_last, 16)
            sp.wait_ge(s_ready, 1)
            sp.dma_start(shared["pen_dram"].rearrange("(c q) e -> q c e", q=P), pen[:]).then_inc(s_out, 16)
            for j in range(4):
                sp.dma_start(row_dram[j].rearrange("(c q) -> q c", q=P), ends[:, j, :],
                             allow_slow_non_contiguous=True).then_inc(s_out, 16)
            sp.wait_ge(s_out, 80)
            sp.dma_start(shared["first_rel"][:, 0:NG], row_dram[3].rearrange("(g k) -> k g", k=GP),
                         allow_slow_non_contiguous=True).then_inc(s_row, 16)
            for j in range(3):
                sp.dma_start(rows[0:1, j, :], row_dram[j:j + 1, :]).then_inc(s_row, 16)
            sp.wait_ge(s_store, 1)
            sp.dma_start(shared["src_dram"][:, 0:NP], idx_e["src"][:]).then_inc(s_out, 16)
            sp.dma_start(shared["rel_dram"][:, 0:NP], idx_e["rel"][:]).then_inc(s_out, 16)
            for k in ("src_dram", "rel_dram"):
                sp.dma_start(shared[k][:, NP:NP + U * GP], pad["src"][:, 0:U * GP]).then_inc(s_out, 16)
            sp.wait_ge(s_lp, 1)
            sp.dma_start(shared["last_dram"], pint[:, 0:NB]).then_inc(s_out, 16)
            sp.wait_ge(s_out, 80 + 80)

        @block.vector
        def _(dve):
            step = [0]

            def link(ins):
                step[0] += 1
                ins.then_inc(s_v, 1)
                dve.wait_ge(s_v, step[0])

            V = nc.vector
            dve.wait_ge(s_iota, 4)
            V.tensor_copy(iota_row[:], iota_i[:])
            V.memset(ones[:], 1.0)
            V.tensor_copy(tile_nf[:], tile_no[:])
            V.tensor_copy(pair_nf[:], pair_no[:])
            link(V.tensor_copy(part_f[:], part_i[:]))
            link(V.tensor_scalar(ident[:], iota_row[:], part_f[:, 0:1], None, ALU.is_equal))
            dve.wait_ge(s_last, 16)
            link(V.tensor_scalar(last_b[:], last_i[:], 7, None, ALU.arith_shift_right))
            link(V.tensor_copy(last_f[:], last_b[:]))
            link(V.tensor_tensor(key[:], last_f[:], tile_nf[:], ALU.add))
            V.tensor_tensor(diag[:], ident[:].unsqueeze(1).to_broadcast([P, NC, P]),
                            key[:].unsqueeze(2).to_broadcast([P, NC, P]), ALU.mult).then_inc(s_keys, 1)
            dve.wait_ge(s_wide, 1)
            wide_flat = wide[:].rearrange("p b f -> p (b f)")[:, 0:NP]
            for c in range(NC):
                link(V.tensor_scalar(junk[:], wide_flat, pair_nf[:, c:c + 1], 0.0, ALU.is_lt, ALU.add,
                                     accum_out=tile_f[:, c:c + 1]))
            link(V.tensor_copy(tile_i[:], tile_f[:]))
            link(V.tensor_tensor(block_f[:], pair_nf[:], tile_f[:], ALU.subtract))
            V.tensor_scalar(block0[:], block_f[:], float(P), None, ALU.mult).then_inc(s_tiles, 1)
            link(V.tensor_tensor(diag[:], ident[:].unsqueeze(1).to_broadcast([P, NC, P]),
                                 last_f[:].unsqueeze(2).to_broadcast([P, NC, P]), ALU.mult))
            V.tensor_copy(ends[:, 2, :], block_f[:]).then_inc(s_keys, 1)
            dve.wait_ge(s_wide, 2)
            link(V.tensor_scalar(junk[:], wide_flat, part_f[:, 0:1], 0.0, ALU.is_le, ALU.add,
                                 accum_out=cnt[:, 0:1]))
            link(V.tensor_tensor(cnt[:], cnt[:], part_f[:], ALU.add))
            V.tensor_scalar(pqf[:], ident[:], cnt[:, 0:1], None, ALU.mult).then_inc(s_keys, 1)
            dve.wait_ge(s_wide, 3)
            link(V.tensor_copy(pint[:], turn[:, 0, 0:P]))
            link(V.tensor_scalar(pq[:], pint[:], 4, None, ALU.arith_shift_right))
            link(V.tensor_copy(pqf[:], pq[:]))
            link(V.tensor_scalar(prf[:], pqf[:], -float(GP), None, ALU.mult))
            link(V.tensor_tensor(prf[:], prf[:], turn[:, 0, 0:P], ALU.add))
            link(V.scalar_tensor_tensor(pqf[:], pqf[:], float(P * GP), prf[:], ALU.mult, ALU.add))
            link(V.tensor_scalar(cnt[:], part_f[:], float(GP), float(P * GP), ALU.mult, ALU.add))
            link(V.tensor_scalar(pqf[:], pqf[:], cnt[:, 0:1], None, ALU.add))
            V.tensor_copy(pint[:], pqf[:]).then_inc(s_lp, 1)
            dve.wait_ge(s_gat, 16 * 3 * NC)
            for k in ("dst", "src", "rel"):
                link(V.tensor_copy(edge_f[k][:], got_i[k][:]))
            d = edge_f["dst"]
            V.tensor_copy(ends[:, 0, :], d[:, :, 0])
            V.tensor_copy(ends[:, 1, :], d[:, :, P - 1])
            link(V.scalar_tensor_tensor(edge_f["rel"][:], edge_f["src"][:], float(R), edge_f["rel"][:],
                                        ALU.mult, ALU.add))
            V.memset(pen[:], -BIG)
            link(V.tensor_tensor(edge_f["la"][:, :, 0:P - 1], d[:, :, 1:P], d[:, :, 0:P - 1], ALU.is_equal))
            link(V.tensor_scalar(pen[:, :, 1:P], edge_f["la"][:, :, 0:P - 1], -1.0, BIG, ALU.add, ALU.mult))
            link(V.tensor_scalar(edge_f["la"][:, :, 0:P - 1], edge_f["la"][:, :, 0:P - 1], -1.0, 1.0,
                                 ALU.mult, ALU.add))
            link(V.memset(edge_f["la"][:, :, P - 1:P], 1.0))
            link(V.tensor_tensor(edge_f["pf"][:], d[:], d[:, :, 0:1].to_broadcast([P, NC, P]), ALU.is_equal))
            link(V.tensor_scalar(edge_f["pf"][:], edge_f["pf"][:], -1.0, BIG, ALU.add, ALU.mult))
            link(V.tensor_tensor(ends[:, 3, :], d[:, :, 0], block0[:], ALU.subtract))
            V.tensor_tensor(d[:], d[:], block0[:].unsqueeze(2).to_broadcast([P, NC, P]),
                            ALU.subtract).then_inc(s_ready, 1)
            n = 0
            target = {"dst": shared["dstrel"], "src": idx_e["src"], "rel": idx_e["rel"],
                      "pf": shared["pen_first"], "la": shared["is_last"]}
            for k in order:
                for c0 in range(0, NC, 4):
                    w = min(4, NC - c0) * P
                    n += 1
                    dve.wait_ge(s_turn, n)
                    V.tensor_copy(target[k][:, c0 * P:c0 * P + w], turn[:, n % 2, 0:w]).then_inc(s_copied, 1)
            link(V.memset(shared["dstrel"][:, NP:NP + 2 * GP], -1.0))
            link(V.memset(shared["first_rel"][:, NG:NG + 2], -1.0))
            dve.wait_ge(s_copied, n)
            V.sem_inc(s_store, 1)
            dve.wait_ge(s_row, 64)
            f, l, b = (rows[0:1, j, :] for j in range(3))
            keep = shared["same_block"]
            link(V.memset(keep[0:1, 0:1], 0.0))
            link(V.tensor_tensor(keep[0:1, 1:NP], b[:, 1:NP], b[:, 0:NP - 1], ALU.is_equal))
            link(V.memset(same[0:1, 0:1], 0.0))
            link(V.tensor_tensor(same[0:1, 1:NP], f[:, 1:NP], l[:, 0:NP - 1], ALU.is_equal))
            link(V.tensor_tensor(same[:], same[:], keep[0:1, 0:NP], ALU.mult))
            link(V.tensor_scalar(shared["pen_cont"][0:1, 0:NP], same[:], -1.0, BIG, ALU.add, ALU.mult))
            link(V.tensor_tensor(blk[:], f, l, ALU.is_equal))
            link(V.tensor_tensor(same[:], same[:], blk[:], ALU.mult))
            link(V.tensor_scalar(shared["pen_chain"][0:1, 0:NP], same[:], -1.0, BIG, ALU.add, ALU.mult))
            link(V.memset(shared["log_reset"][0:1, 0:GP], LOGMIN))
            link(V.memset(shared["ones_b"][:], 1.0))
            link(V.tensor_copy(shared["ident_b"][:], ident[:]))
            link(V.tensor_scalar(shared["log_reset"][0:1, GP:GP + NP], keep[0:1, 0:NP], -1.0, -LOGMIN, ALU.add, ALU.mult))
            link(V.tensor_scalar(blk[:], b, float(NB - 1), float(DW), ALU.min, ALU.mult))
            link(V.memset(shared["block_at"][0:1, NP:NP + GP], 0))
            link(V.tensor_copy(shared["block_at"][0:1, 0:NP], blk[:]))

        @block.tensor
        def _(pe):
            def spread():
                for c in range(NC):
                    mm = pe.matmul(wide[:, c // 4, (c % 4) * P:(c % 4 + 1) * P], ones[:], diag[:, c, :],
                                   start=True, stop=True)
                mm.then_inc(s_wide, 1)
            pe.wait_ge(s_keys, 1)
            spread()
            pe.wait_ge(s_keys, 2)
            spread()
            pe.wait_ge(s_keys, 3)
            pe.matmul(turn[:, 0, 0:P], ones[:], pqf[:], start=True, stop=True).then_inc(s_wide, 1)
            pe.wait_ge(s_lp, 1)
            pe.wait_ge(s_ready, 1)
            n = 0
            for k in order:
                for c0 in range(0, NC, 4):
                    n += 1
                    if n > 2:
                        pe.wait_ge(s_copied, n - 2)
                    for c in range(c0, min(c0 + 4, NC)):
                        mm = pe.transpose(turn[:, n % 2, (c - c0) * P:(c - c0 + 1) * P], edge_f[k][:, c, :],
                                          ident[:])
                    mm.then_inc(s_turn, 1)


def weights_phase(nc, top, inputs, sh):
    s_in = top.sem("w_in")
    s_v = top.sem("w_vector_step")
    s_col = top.sem("w_vectors_spread")
    s_pe = top.sem("w_tensor")
    s_cp = top.sem("w_copied")
    with ExitStack() as ctx:
        col = ctx.enter_context(nc.sbuf_tensor("attn_col", [D, 6], F32))
        mask = ctx.enter_context(nc.sbuf_tensor("head_mask", [D, H], F32))
        mask1 = ctx.enter_context(nc.sbuf_tensor("head_mask1", [D, H], F32))
        spread = ctx.enter_context(nc.sbuf_tensor("attn_spread", [D, 6, H], F32))
        wt = ctx.enter_context(nc.sbuf_tensor("w_turned", [D, 3, D], F32))
        tp = ctx.enter_context(nc.psum_tensor("w_turn", [D, 512], F32))
        up = ctx.enter_context(nc.psum_tensor("w_scores", [D, 512], F32))
        block = ctx.enter_context(nc.Block())
        wx, bias, w4 = sh["wx"], sh["bias"], sh["w4"]

        @block.sync
        def _(sp):
            n = 0
            for l in range(3):
                sp.dma_start(wx[:, l, 0:D], inputs[f"L0_gnn_W{l + 1}"]).then_inc(s_in, 16)
                for j, side in enumerate(("src", "dst")):
                    a = inputs[f"L0_gnn_a{l + 1}_{side}"].rearrange("h (c u) -> (h c) u", u=1)
                    sp.dma_start(col[:, 2 * l + j:2 * l + j + 1], a).then_inc(s_in, 16)
                b = inputs[f"L0_gnn_b{l + 1}"].rearrange("(u f) -> u f", u=1)
                sp.dma_start(bias[:, l, :], b.to_broadcast([P, D])).then_inc(s_in, 16)
                n += 4
            sp.dma_start(w4[:], inputs["L1_gnn_weight"].rearrange("r i o -> i r o")).then_inc(s_in, 16)

        @block.vector
        def _(dve):
            V = nc.vector
            step = [0]

            def link(ins):
                step[0] += 1
                ins.then_inc(s_v, 1)
                dve.wait_ge(s_v, step[0])

            link(V.tensor_scalar(mask1[:], sh["iota_row"][0:D, 0:H], -float(C), None, ALU.mult))
            link(V.tensor_scalar(mask[:], mask1[:], sh["part_f"][0:D, 0:1], None, ALU.add))
            link(V.tensor_scalar(mask1[:], mask[:], 0.0, None, ALU.is_ge))
            link(V.scalar_tensor_tensor(mask[:], mask[:], float(C - 1), mask1[:], ALU.is_le, ALU.mult))
            dve.wait_ge(s_in, 16 * 13)
            for j in range(4):
                V.tensor_scalar(spread[:, j, :], mask[:], col[:, j:j + 1], None, ALU.mult).then_inc(s_col, 1)
            for j in range(4, 6):
                V.tensor_scalar(spread[:, j, :], sh["ones"][0:D, 0:H], col[:, j:j + 1], None,
                                ALU.mult).then_inc(s_col, 1)
            dve.wait_ge(s_pe, 1)
            V.tensor_copy(wt[:].rearrange("p l f -> p (l f)"), tp[:, 0:3 * D]).then_inc(s_cp, 1)
            dve.wait_ge(s_pe, 2)
            V.tensor_copy(wx[:, :, D:XW], up[:, 0:48].rearrange("p (l f) -> p l f", l=3)).then_inc(s_cp, 1)

        @block.tensor
        def _(pe):
            pe.wait_ge(s_in, 16 * 13)
            for l in range(3):
                mm = pe.transpose(tp[:, l * D:(l + 1) * D], wx[:, l, 0:D], sh["ident"][0:D, 0:D])
            mm.then_inc(s_pe, 1)
            pe.wait_ge(s_cp, 1)
            pe.wait_ge(s_col, 6)
            for l in range(3):
                mm = pe.matmul(up[:, 16 * l:16 * l + 16], wt[:, l, :],
                               spread[:, 2 * l:2 * l + 2, :].rearrange("p j h -> p (j h)"), start=True, stop=True)
            mm.then_inc(s_pe, 1)


def node_phase(nc, top, sh, kind, layer, x=None, sums=None, table=None):
    tag = f"n{layer}_"
    attn = kind != "first"
    norm = kind != "next"
    maps = kind != "relations"
    BH = CB * H
    steps = {"first": 9, "next": 14, "relations": 21}[kind]
    asks = attn + (kind == "next") + norm
    s = {n: top.sem(tag + n) for n in ("vector_step", "x_zeroed", "x_in", "asked", "answered", "h_ready", "turned",
                                       "ht_copied", "mapped", "rows_copied", "used", "stored", "spare")}
    s_idx = [top.sem(tag + f"index_in{h}") for h in range(2)]
    s_ac = [top.sem(tag + f"sums_in{h}") for h in range(2)]
    s_wr = [top.sem(tag + f"written{h}") for h in range(2)]
    res, xp, wx = sh["res"], sh["xp"], sh["wx"]
    whole = N // P
    with ExitStack() as ctx:
        sb = lambda n, sh_, d=F32: ctx.enter_context(nc.sbuf_tensor(tag + n, sh_, d))
        li = sb("sum_rows", [P, 2, CB], I32)
        ac = sb("sums", [P, 2, CB, SW])
        hc = sb("hidden", [P, 2, CB, D])
        t1 = sb("t1", [P, CB, D])
        t2 = sb("t2", [P, CB, D])
        zs = sb("self_score", [P, BH])
        mx = sb("edge_max", [P, BH])
        mt = sb("all_max", [P, BH])
        ex = sb("exps", [P, 2, BH])
        dn = sb("denominator", [P, BH])
        st = sb("stat", [P, 4, CB])
        ht = sb("hidden_turned", [D, CB * P])
        wide = sb("relation_rows", [P, 2, R * D])
        turn = ctx.enter_context(nc.psum_tensor(tag + "turn", [P, 2, 512], F32))
        prod = ctx.enter_context(nc.psum_tensor(tag + "prod", [P, 4, 512], F32))
        block = ctx.enter_context(nc.Block())
        V, A = nc.vector, nc.scalar

        def chunk(k, w):
            return bass.ds(k * (CB * w), CB * w)

        def flat(ap):
            return ap.rearrange("p b f -> p (b f)")

        def by_head(ap):
            return ap.rearrange("p (b h) -> p b h", b=CB)

        @block.vector
        def _(dve):
            V.sem_inc(s["used"], 2)
            if kind == "first":
                V.memset(res[:, whole * D:NB * D], 0.0).then_inc(s["x_zeroed"], 1)
                dve.wait_ge(s["x_in"], 32)
            with dve.Fori(0, NCH // 2) as i:
                for h in range(2):
                    k = i * 2 + h
                    n = [0, 0]

                    def link(ins):
                        n[0] += 1
                        ins.then_inc(s["vector_step"], 1)
                        dve.wait_ge(s["vector_step"], k * steps + n[0])

                    def ask(ins):
                        n[1] += 1
                        ins.then_inc(s["asked"], 1)
                        dve.wait_ge(s["answered"], k * asks + n[1])

                    rk, hk = res[:, chunk(k, D)], hc[:, h]
                    if attn:
                        dve.wait_ge(s_ac[h], i * (16 * CB) + 16 * CB)
                        a = ac[:, h]
                        xk = xp[:, chunk(k, XW)].rearrange("p (b f) -> p b f", b=CB)
                        split = lambda ap: ap.rearrange("p b (h c) -> p b h c", h=H)
                        weight = lambda j: by_head(ex[:, j, :]).unsqueeze(3).to_broadcast([P, CB, H, C])
                        link(V.tensor_tensor(by_head(zs[:]), xk[:, :, D:TW], xk[:, :, TW:XW], ALU.add))
                        V.tensor_scalar(by_head(mx[:]), a[:, :, D:D + H], 0.0, -BIG, ALU.is_equal, ALU.mult)
                        link(V.scalar_tensor_tensor(zs[:], zs[:], 0.2, zs[:], ALU.mult, ALU.max))
                        link(V.tensor_tensor(by_head(mx[:]), by_head(mx[:]), a[:, :, TW:SW], ALU.add))
                        link(V.tensor_tensor(mt[:], mx[:], zs[:], ALU.max))
                        link(V.tensor_tensor(ex[:, 0, :], mx[:], mt[:], ALU.subtract))
                        ask(V.tensor_tensor(ex[:, 1, :], zs[:], mt[:], ALU.subtract))
                        link(V.tensor_tensor(by_head(dn[:]), by_head(ex[:, 0, :]), a[:, :, D:D + H], ALU.mult))
                        link(V.tensor_tensor(dn[:], dn[:], ex[:, 1, :], ALU.add))
                        link(V.tensor_scalar(dn[:], dn[:], 1e-16, None, ALU.add))
                        link(V.reciprocal(dn[:], dn[:]))
                        link(V.tensor_tensor(ex[:], ex[:], dn[:].unsqueeze(1).to_broadcast([P, 2, BH]), ALU.mult))
                        V.tensor_tensor(split(t1[:]), split(a[:, :, 0:D]), weight(0), ALU.mult).then_inc(s["used"], 1)
                        link(V.tensor_tensor(split(t2[:]), split(xk[:, :, 0:D]), weight(1), ALU.mult))
                        link(V.tensor_tensor(t1[:], t1[:], t2[:], ALU.add))
                        link(V.tensor_tensor(t1[:], t1[:], sh["bias"][:, layer - 1, :].unsqueeze(1)
                                             .to_broadcast([P, CB, D]), ALU.add))
                    dve.wait_ge(s["turned"], k + 1)
                    if kind == "next":
                        ask(V.tensor_scalar(t2[:], t1[:], 0.0, None, ALU.min))
                        link(V.tensor_scalar(t1[:], t1[:], 0.0, None, ALU.max))
                        V.scalar_tensor_tensor(hk, t2[:], -1.0, t1[:], ALU.add, ALU.add).then_inc(s["h_ready"], 1)
                    if kind == "relations":
                        link(V.tensor_tensor(flat(t1[:]), flat(t1[:]), rk, ALU.add))
                        V.tensor_scalar(rk, flat(t1[:]), 1.0, None, ALU.mult)
                    if norm:
                        if kind == "first":
                            link(V.tensor_scalar(flat(t1[:]), rk, 1.0, None, ALU.mult))
                        xin = t1[:]
                        per_node = lambda j: st[:, j, :].unsqueeze(2).to_broadcast([P, CB, D])
                        link(V.tensor_reduce(st[:, 0, :], xin, AX.X, ALU.add))
                        link(V.tensor_scalar(st[:, 1, :], st[:, 0, :], 1.0 / D, None, ALU.mult))
                        link(V.tensor_tensor(t2[:], xin, per_node(1), ALU.subtract))
                        link(V.tensor_tensor(hk, t2[:], t2[:], ALU.mult))
                        link(V.tensor_reduce(st[:, 2, :], hk, AX.X, ALU.add))
                        ask(V.tensor_scalar(st[:, 2, :], st[:, 2, :], 1.0 / D, 1e-5, ALU.mult, ALU.add))
                        link(V.reciprocal(st[:, 3, :], st[:, 3, :]))
                        link(V.tensor_tensor(t2[:], t2[:], per_node(3), ALU.mult))
                        relu = V.tensor_scalar(hk, t2[:], 0.0, None, ALU.max)
                        if kind == "first":
                            link(relu)
                            relu = V.tensor_tensor(rk, rk, flat(hk), ALU.add)
                        relu.then_inc(s["h_ready"], 1)
                    assert n == [steps, asks], (kind, n)

        @block.gpsimd
        def _(pool):
            if not attn:
                return
            with pool.Fori(0, NCH // 2) as i:
                for h in range(2):
                    pool.wait_ge(s_idx[h], i * 16 + 16)
                    pool.nop(nofuse=True)
                    pool.wait_ge(s["used"], i * 2 + (h + 1))
                    pool.nop(nofuse=True)
                    for b in range(CB):
                        nc.gpsimd.indirect_dma_start(
                            out=ac[:, h, b, :], out_offset=None, in_=sums,
                            in_offset=bass.IndirectOffsetOnAxis(ap=li[:, h, b:b + 1], axis=0)).then_inc(s_ac[h], 16)

        @block.sync
        def _(sp):
            if not attn:
                sp.wait_ge(s["x_zeroed"], 1)
                sp.dma_start(res[:, 0:whole * D].rearrange("p (b f) -> p b f", f=D),
                             x[0:whole * P, :].rearrange("(b n) f -> n b f", n=P)).then_inc(s["x_in"], 16)
                sp.dma_start(res[0:N - whole * P, whole * D:NB * D], x[whole * P:N, :]).then_inc(s["x_in"], 16)
            if not maps:
                for q in range(2):
                    sp.dma_start(sh["spare"][:, q, :], sh["ones"][:]).then_inc(s_wr[q], 16)
            with sp.Fori(0, NCH // 2) as i:
                for h in range(2):
                    k = i * 2 + h
                    if attn:
                        sp.wait_ge(s["used"], k + 1)
                        sp.dma_start(li[:, h, :], sh["last_dram"][:, bass.ds(k * CB, CB)]).then_inc(s_idx[h], 16)
                    if maps:
                        sp.wait_ge(s["rows_copied"], k + 1)
                        rows = xp[:, chunk(k, XW)].rearrange("p (b f) -> p b f", b=CB)[:, :, 0:TW]
                        sp.dma_start(table.rearrange("(b n) f -> n b f", n=P)[:, bass.ds(k * CB, CB), :],
                                     rows).then_inc(s["stored"], 16)
                        continue
                    for b in range(CB):
                        m, q = k * CB + b, (CB * h + b) % 2
                        sp.wait_ge(s["rows_copied"], m + 3)
                        sp.dma_start(table.rearrange("(b n r) f -> n b (r f)", n=P, r=R)[:, bass.ds(m, 1), :],
                                     wide[:, q:q + 1, :]).then_inc(s_wr[q], 16)
            if maps:
                sp.wait_ge(s["stored"], 16 * NCH)
            else:
                for q in range(2):
                    sp.wait_ge(s_wr[q], 16 * (NB // 2 + 1))

        @block.scalar
        def _(act):
            if not maps:
                A.sem_inc(s["rows_copied"], 2)
            with act.Fori(0, NCH // 2) as i:
                for h in range(2):
                    k = i * 2 + h
                    n = [0]

                    def asked():
                        n[0] += 1
                        act.wait_ge(s["asked"], k * asks + n[0])

                    if attn:
                        asked()
                        A.activation(ex[:], ex[:], ACT.Exp).then_inc(s["answered"], 1)
                    if kind == "next":
                        asked()
                        A.activation(t2[:], t2[:], ACT.Exp).then_inc(s["answered"], 1)
                    if norm:
                        asked()
                        A.activation(st[:, 3, :], st[:, 2, :], ACT.Sqrt).then_inc(s["answered"], 1)
                    act.wait_ge(s["turned"], k + 3)
                    A.copy(ht[:, 0:4 * P], turn[0:D, 0, 0:4 * P])
                    A.copy(ht[:, 4 * P:CB * P], turn[0:D, 1, 0:3 * P]).then_inc(s["ht_copied"], 1)
                    if maps:
                        act.wait_ge(s["mapped"], k + 1)
                        o = xp[:, chunk(k, XW)]
                        A.copy(o[:, 0:4 * XW], prod[:, 0, 0:4 * XW])
                        A.copy(o[:, 4 * XW:CB * XW], prod[:, 1, 0:3 * XW]).then_inc(s["rows_copied"], 1)
                        continue
                    for b in range(CB):
                        m, q = k * CB + b, (CB * h + b) % 2
                        act.wait_ge(s["mapped"], m + 1)
                        act.wait_ge(s_wr[q], i * (16 * CB) + 16 * ((CB * h + b) // 2 + 1))
                        A.copy(wide[:, q, 0:512], prod[:, 2 * q, :])
                        A.copy(wide[:, q, 512:1024], prod[:, 2 * q + 1, :]).then_inc(s["rows_copied"], 1)

        @block.tensor
        def _(pe):
            pe.sem_inc(s["turned"], 2)
            with pe.Fori(0, NCH // 2) as i:
                for h in range(2):
                    k = i * 2 + h
                    pe.wait_ge(s["h_ready"], k + 1)
                    pe.nop(nofuse=True)
                    for b in range(CB):
                        mm = pe.transpose(turn[0:D, b // 4, (b % 4) * P:(b % 4 + 1) * P], hc[:, h, b, :], sh["ident"][:])
                    mm.then_inc(s["turned"], 1)
                    pe.wait_ge(s["ht_copied"], k + 1)
                    for b in range(CB):
                        lhs = ht[:, b * P:(b + 1) * P]
                        if maps:
                            mm = pe.matmul(prod[:, b // 4, (b % 4) * XW:(b % 4 + 1) * XW], lhs, wx[:, layer, :],
                                           start=True, stop=True)
                            continue
                        m, q = k * CB + b, (CB * h + b) % 2
                        w = sh["w4"][:].rearrange("p r f -> p (r f)")
                        pe.wait_ge(s["rows_copied"], m + 1)
                        pe.matmul(prod[:, 2 * q, :], lhs, w[:, 0:512], start=True, stop=True)
                        pe.matmul(prod[:, 2 * q + 1, :], lhs, w[:, 512:1024], start=True, stop=True)\
                          .then_inc(s["mapped"], 1)
                    if maps:
                        mm.then_inc(s["mapped"], 1)


def attention_edges(nc, top, sh, layer, table, sums):
    tag = f"g{layer}_"
    CR = 4
    s = {n: top.sem(tag + n) for n in (
        "vector_step", "z_done", "oh_done", "zt_done", "ml_done", "rows_done", "carry_done", "log_done", "bc_done",
        "log_spread", "diag_done", "cut_done", "hi_done", "left_done", "mid_done", "parts_done",
        "zz_done", "p_done", "msg_done", "sum_done", "scan_done", "oht_turned", "oht_copied", "d_done",
        "lf_done", "f_done", "s1_done", "out_copied")}
    s_idx = [top.sem(tag + f"index_in{u}") for u in range(U)]
    s_pen = [top.sem(tag + f"pen_in{u}") for u in range(U)]
    s_got = [top.sem(tag + f"rows_in{u}") for u in range(U)]
    s_wr = [top.sem(tag + f"written{u}") for u in range(U)]
    STEPS = 7
    GH = GP * H
    with ExitStack() as ctx:
        sb = lambda n, sh_, d=F32: ctx.enter_context(nc.sbuf_tensor(tag + n, sh_, d))
        ps = lambda n, sh_: ctx.enter_context(nc.psum_tensor(tag + n, sh_, F32))
        idx = sb("index", [P, U, GP], I32)
        pen = sb("pen", [P, 2, P + 1])
        rows = sb("rows", [P, U, GP, TW])
        onehot = sb("onehot", [P, U, GP * P], BF16)
        onehot_t = sb("onehot_turned", [P, GP * P], BF16)
        first_oh = sb("first_onehot", [GP, U, P])
        targ = sb("target_parts", [P, NB, DW], BF16)
        cut = sb("target_left", [P, NB, H])
        z = sb("score", [P, 2, GH])
        fw = sb("max_forward", [P, P])
        ml = sb("max_local", [P, P])
        tm = sb("tmp_max", [P, GH])
        mm_ = sb("edge_max", [P, GH])
        zz = sb("score_less_max", [P, 2, GH])
        msg = sb("messages", [P, GP, SW])
        parts = sb("message_parts", [P, 3, GP, SW], BF16)
        factor = sb("factor", [P, SW, GP + 1])
        part = sb("part", [P, SW, GP + 1])
        total = sb("total", [P, SW, GP + 1])
        outm = sb("sums_by_pair", [P, 2, GP, SW])
        lx = sb("chain_in", [1, H, GP + 1])
        px = sb("chain_pen", [1, H, GP + 1])
        ch = sb("chain", [1, H, GP + 1])
        cm = sb("carry", [1, GP, H])
        lg = sb("log_factor", [1, GH])
        lgd = sb("log_factor_diagonal", [GP, GP, 2 * H])
        p_part = ps("p_part", [P, 3, 512])
        p_turn = ctx.enter_context(nc.psum_tensor(tag + "p_turn", [P, 2, 8 * P], BF16))
        p_logf = ps("p_logf", [P, 512])
        p_a = ps("p_a", [P, 512])
        p_b = ps("p_b", [P, 512])
        d_e, z_t = p_a[:, 0:GH], p_a[:, GH:2 * GH]
        m_t, b_c, r_l, b_l = (p_b[0:n, j * GH:(j + 1) * GH] for j, n in enumerate((P, P, 1, P)))
        block = ctx.enter_context(nc.Block())
        V, A = nc.vector, nc.scalar
        pairs = lambda ap: ap.rearrange("p (k h) -> p k h", k=GP)
        flat3 = lambda ap: ap.rearrange("p k h -> p (k h)")

        @block.gpsimd
        def _(pool):
            with pool.Fori(0, NG // U) as i:
                for u in range(U):
                    pool.wait_ge(s_idx[u], i * 16 + 16)
                    pool.nop(nofuse=True)
                    pool.wait_ge(s["msg_done"], i * U + (u + 1))
                    pool.nop(nofuse=True)
                    for k in range(GP):
                        nc.gpsimd.indirect_dma_start(
                            out=rows[:, u, k, :], out_offset=None, in_=table,
                            in_offset=bass.IndirectOffsetOnAxis(ap=idx[:, u, k:k + 1], axis=0)).then_inc(s_got[u], 16)

        @block.sync
        def _(sp):
            sp.wait_ge(s["out_copied"], CR)
            for u in (2, 3):
                sp.dma_start(sums_rows(sums, NG + u - 1), outm[:, u % 2].rearrange("p k f -> p (k f)"))\
                  .then_inc(s_wr[u], 16)
            for u in range(U - 1):
                sp.dma_start(idx[:, u, :], sh["src_dram"][:, u * GP:(u + 1) * GP]).then_inc(s_idx[u], 16)
            with sp.Fori(0, NG // U) as i:
                for u in range(U):
                    g, ahead = i * U + u, (u + U - 1) % U
                    sp.wait_ge(s["z_done"], g + CR)
                    sp.dma_start(idx[:, ahead, :],
                                 sh["src_dram"][:, bass.ds((g + (U - 1)) * GP, GP)]).then_inc(s_idx[ahead], 16)
                    sp.wait_ge(s["ml_done"], g + (CR - 1))
                    pen_rows = sh["pen_dram"].rearrange("(g k) (h e) -> g k h e", k=GP, h=1)
                    sp.dma_start(pen[:, u % 2, :], pen_rows[bass.ds(g, 1)].rearrange("g k h e -> (g k) h e")
                                 .to_broadcast([GP, H, P + 1])).then_inc(s_pen[u], 16)
                    sp.wait_ge(s["out_copied"], g + (CR + 1))
                    sp.dma_start(sums_rows(sums, g), outm[:, (u + 1) % 2].rearrange("p k f -> p (k f)"))\
                      .then_inc(s_wr[u], 16)
            sp.wait_ge(s["out_copied"], NG + CR + 1)
            sp.dma_start(sums_rows(sums, NG), outm[:, (NG + 1) % 2].rearrange("p k f -> p (k f)"))\
              .then_inc(s_wr[0], 16)
            for u in range(U):
                sp.wait_ge(s_wr[u], 16 * (NG // U + (u != 1)))
                sp.wait_ge(s_idx[u], 16 * (NG // U + (u < U - 1)))

        @block.vector
        def _(dve):
            def one_hot(g, half):
                V.tensor_tensor(onehot[:, half, :].rearrange("p (k n) -> p k n", k=GP),
                                sh["iota_row"][:].unsqueeze(1).to_broadcast([P, GP, P]),
                                sh["dstrel"][:, bass.ds(g * GP, GP)].unsqueeze(2).to_broadcast([P, GP, P]),
                                ALU.is_equal)
                V.tensor_scalar(first_oh[:, half, :], sh["iota_row"][0:GP, :], sh["first_rel"][:, bass.ds(g, 1)], None,
                                ALU.is_equal).then_inc(s["oh_done"], 1)

            def scan_sums():
                V.tensor_tensor_scan(total[:].rearrange("p f k -> p (f k)"), factor[:].rearrange("p f k -> p (f k)"),
                                     part[:].rearrange("p f k -> p (f k)"), 0.0, ALU.mult, ALU.add)\
                 .then_inc(s["scan_done"], 1)

            V.memset(parts[:], 0.0).then_inc(s["parts_done"], 1)
            V.memset(onehot[:, U - 1, :], 0.0)
            V.memset(first_oh[:, U - 1, :], 0.0)
            V.memset(lgd[:, :, 0:H], 0.0).then_inc(s["diag_done"], 1)
            V.memset(factor[:], 0.0)
            V.memset(part[:], 0.0)
            V.memset(total[:], 0.0)
            V.memset(ch[:], -BIG)
            V.memset(px[:], -BIG)
            V.tensor_scalar(lgd[:, :, H:2 * H], sh["ident"][0:GP, 0:GP].unsqueeze(2).to_broadcast([GP, GP, H]), LOGMIN,
                            None, ALU.mult)
            score = sh["xp"][:].rearrange("p (b f) -> p b f", f=XW)[:, :, TW:XW]
            V.tensor_copy(targ[:, :, 0:H], score).then_inc(s["cut_done"], 1)
            for j in (1, 2):
                dve.wait_ge(s["cut_done"], 2 * j - 1)
                V.tensor_tensor(cut[:], score if j == 1 else cut[:], targ[:, :, (j - 1) * H:j * H],
                                ALU.subtract).then_inc(s["cut_done"], 1)
                dve.wait_ge(s["cut_done"], 2 * j)
                V.tensor_copy(targ[:, :, j * H:(j + 1) * H], cut[:]).then_inc(s["cut_done"], 1)
            V.memset(outm[:], 0.0).then_inc(s["out_copied"], CR)
            for name in ("msg_done", "z_done", "ml_done", "oh_done", "zz_done", "scan_done", "carry_done", "log_done",
                         "f_done", "s1_done"):
                V.sem_inc(s[name], CR)
            one_hot(0, 0)
            one_hot(1, 1)
            with dve.Fori(0, NG // U) as i:
                for u in range(U):
                    g, y = i * U + u, u % 2
                    n = [0]

                    def link(ins):
                        n[0] += 1
                        ins.then_inc(s["vector_step"], 1)
                        dve.wait_ge(s["vector_step"], g * STEPS + n[0])

                    at = bass.ds(g * GP, GP)
                    dve.wait_ge(s_got[u], i * (16 * GP) + 16 * GP)
                    dve.wait_ge(s["d_done"], g + 1)
                    link(V.tensor_tensor(pairs(z[:, y, :]), rows[:, u, :, D:TW], pairs(d_e), ALU.add))
                    V.scalar_tensor_tensor(z[:, y, :], z[:, y, :], 0.2, z[:, y, :], ALU.mult, ALU.max)\
                     .then_inc(s["z_done"], 1)
                    dve.wait_ge(s["zt_done"], g + 1)
                    dve.wait_ge(s_pen[u], i * 16 + 16)
                    link(V.tensor_tensor_scan(fw[:], pen[:, y, 0:P], z_t, -BIG, ALU.add, ALU.max))
                    V.tensor_tensor_scan(ml[:, ::-1], pen[:, y, P:0:-1], fw[:, ::-1], -BIG, ALU.add, ALU.max)\
                     .then_inc(s["ml_done"], 1)
                    one_hot(g + 2, (u + 2) % U)
                    dve.wait_ge(s["rows_done"], g + 1)
                    V.tensor_copy(lx[:, :, 1:GP + 1], pairs(r_l).rearrange("p k h -> p h k"))
                    V.tensor_copy(lx[:, :, 0:1], ch[:, :, GP:GP + 1])
                    link(V.tensor_copy(px[:, :, 1:GP + 1],
                                       sh["pen_chain"][0:1, at].unsqueeze(1).to_broadcast([1, H, GP])))
                    link(V.tensor_tensor_scan(ch[:].rearrange("p h k -> p (h k)"), px[:].rearrange("p h k -> p (h k)"),
                                              lx[:].rearrange("p h k -> p (h k)"), -BIG, ALU.add, ALU.max))
                    dve.wait_ge(s["bc_done"], g + 1)
                    V.tensor_tensor(cm[:], ch[:, :, 0:GP].rearrange("p h k -> p k h"),
                                    sh["pen_cont"][0:1, at].unsqueeze(2).to_broadcast([1, GP, H]),
                                    ALU.add).then_inc(s["carry_done"], 1)
                    dve.wait_ge(s["bc_done"], g + 2)
                    link(V.tensor_tensor(pairs(tm[:]), pairs(b_c),
                                         sh["pen_first"][:, at].unsqueeze(2).to_broadcast([P, GP, H]), ALU.add))
                    link(V.tensor_tensor(mm_[:], tm[:], m_t, ALU.max))
                    V.tensor_tensor(zz[:, y, :], z[:, y, :], mm_[:], ALU.subtract).then_inc(s["zz_done"], 1)
                    V.tensor_tensor(msg[:, :, TW:SW], pairs(mm_[:]),
                                    sh["is_last"][:, at].unsqueeze(2).to_broadcast([P, GP, H]), ALU.mult)
                    dve.wait_ge(s["log_spread"], g + 1)
                    link(V.tensor_tensor(lg[:], flat3(cm[:]), mm_[0:1, :], ALU.subtract))
                    V.tensor_scalar(lg[:], lg[:], LOGMIN, None, ALU.max).then_inc(s["log_done"], 1)
                    dve.wait_ge(s["p_done"], g + 1)
                    V.tensor_tensor(msg[:, :, 0:D].rearrange("p k (h c) -> p k h c", h=H),
                                    rows[:, u, :, 0:D].rearrange("p k (h c) -> p k h c", h=H),
                                    msg[:, :, D:TW].unsqueeze(3).to_broadcast([P, GP, H, C]),
                                    ALU.mult).then_inc(s["msg_done"], 1)
                    dve.wait_ge(s["f_done"], g + (CR + 1))
                    dve.wait_ge(s["s1_done"], g + (CR + 1))
                    scan_sums()
                    dve.wait_ge(s["hi_done"], g + 1)
                    V.tensor_tensor(flat3(msg[:]), flat3(msg[:]), flat3(parts[:, 0]),
                                    ALU.subtract).then_inc(s["left_done"], 1)
                    dve.wait_ge(s["log_spread"], g + 2)
                    V.tensor_tensor(lgd[:, :, 0:H], pairs(b_l[0:GP, :]),
                                    sh["ident"][0:GP, 0:GP].unsqueeze(2).to_broadcast([GP, GP, H]),
                                    ALU.mult).then_inc(s["diag_done"], 1)
                    dve.wait_ge(s["mid_done"], g + 1)
                    V.tensor_tensor(flat3(parts[:, 2]), flat3(msg[:]), flat3(parts[:, 1]),
                                    ALU.subtract).then_inc(s["parts_done"], 1)
                    assert n[0] == STEPS, n
            dve.wait_ge(s["f_done"], NG + CR + 1)
            dve.wait_ge(s["s1_done"], NG + CR + 1)
            scan_sums()

        @block.tensor
        def _(pe):
            ident, ones = sh["ident"], sh["ones"]
            targ_flat = targ[:].rearrange("p b f -> p (b f)")

            def turn_onehots(g, half):
                pe.wait_ge(s["oh_done"], g + (CR + 1))
                for q in range(2):
                    pe.wait_ge(s["oht_copied"], g * 2 + (q + 1))
                    for k in range(8):
                        mm = pe.transpose(p_turn[:, q, k * P:(k + 1) * P],
                                          onehot[:, half, (8 * q + k) * P:(8 * q + k + 1) * P], sh["ident_b"][:])
                    mm.then_inc(s["oht_turned"], 1)

            def spread_targets(g):
                pe.wait_ge(s["oht_copied"], g * 2 + 4)
                _, at = nc.values_load_multi_w_load_instructions(
                    sh["block_at"][0:1, bass.ds(g * GP, GP)], engines=(mybir.EngineType.PE,), min_val=0,
                    max_val=(NB - 1) * DW, skip_runtime_bounds_check_because="the index phase limits it to the last block")
                for k in range(GP):
                    for j in range(3):
                        mm = pe.matmul(d_e[:, k * H:(k + 1) * H], onehot_t[:, k * P:(k + 1) * P],
                                       targ_flat[:, bass.ds(at[k] + j * H, H)], start=(j == 0), stop=(j == 2))
                mm.then_inc(s["d_done"], 1)

            def log_factors(g, half):
                pe.wait_ge(s["f_done"], g + CR)
                pe.matmul(p_logf[:, 0:2 * GH].rearrange("p (k f) -> p k f", k=GP), sh["ones_b"][:],
                          sh["log_reset"][0:1, bass.ds(g * GP, GP)].unsqueeze(2).to_broadcast([1, GP, 2 * H]),
                          start=True, stop=True)
                pe.wait_ge(s["diag_done"], g + 1)
                pe.matmul(p_logf[:, 0:2 * GH], first_oh[:, half, :], lgd[:].rearrange("p k f -> p (k f)"), start=False,
                          stop=True, skip_group_check=True).then_inc(s["lf_done"], 1)

            def node_sums(g, half):
                pe.wait_ge(s["parts_done"], g + 1)
                pe.wait_ge(s["s1_done"], g + CR)
                for k in range(GP):
                    for j in range(3):
                        mm = pe.matmul(p_part[:, k // 6, (k % 6) * SW:(k % 6 + 1) * SW],
                                       onehot[:, half, k * P:(k + 1) * P], parts[:, j, k, :],
                                       start=(j == 0), stop=(j == 2))
                mm.then_inc(s["sum_done"], 1)

            pe.sem_inc(s["bc_done"], 1)
            pe.sem_inc(s["log_spread"], 1)
            pe.wait_ge(s["cut_done"], 5)
            turn_onehots(0, 0)
            spread_targets(0)
            with pe.Fori(0, NG // U) as i:
                for u in range(U):
                    g, y = i * U + u, u % 2
                    pe.wait_ge(s["z_done"], g + (CR + 1))
                    pe.transpose(z_t, z[:, y, :], ident[:]).then_inc(s["zt_done"], 1)
                    log_factors(g, (u + U - 1) % U)
                    pe.wait_ge(s["ml_done"], g + (CR + 1))
                    pe.wait_ge(s["zz_done"], g + CR)
                    pe.transpose(m_t, ml[:], ident[:])
                    pe.transpose(r_l, ml[:, P - 1:P], ident[:]).then_inc(s["rows_done"], 1)
                    node_sums(g, (u + U - 1) % U)
                    pe.wait_ge(s["carry_done"], g + (CR + 1))
                    pe.matmul(b_c, ones[0:1, :], flat3(cm[:]), start=True, stop=True).then_inc(s["bc_done"], 1)
                    turn_onehots(g + 1, (u + 1) % U)
                    pe.wait_ge(s["log_done"], g + (CR + 1))
                    pe.matmul(b_l, ones[0:1, :], lg[:], start=True, stop=True).then_inc(s["log_spread"], 1)
                    spread_targets(g + 1)
            log_factors(NG, U - 1)
            node_sums(NG, U - 1)

        @block.scalar
        def _(act):
            def copy_onehots(g):
                for q in range(2):
                    act.wait_ge(s["oht_turned"], g * 2 + (q + 1))
                    A.copy(onehot_t[:, 8 * q * P:(8 * q + 8) * P], p_turn[:, q, :]).then_inc(s["oht_copied"], 1)

            def factors(g):
                act.wait_ge(s["lf_done"], g + 1)
                lf = p_logf[:, 0:2 * GH].rearrange("p (k f) -> p f k", k=GP)
                A.activation(factor[:, 0:D, 1:GP + 1].rearrange("p (h c) k -> p h c k", h=H),
                             lf[:, 0:H, :].unsqueeze(2).to_broadcast([P, H, C, GP]), ACT.Exp)
                A.activation(factor[:, D:SW, 1:GP + 1], lf, ACT.Exp).then_inc(s["f_done"], 1)

            def copy_parts(g):
                act.wait_ge(s["sum_done"], g + 1)
                for b in range(3):
                    w = min(6, GP - 6 * b)
                    c = A.copy(part[:, :, 1 + 6 * b:1 + 6 * b + w],
                               p_part[:, b, 0:w * SW].rearrange("p (k f) -> p f k", k=w))
                c.then_inc(s["s1_done"], 1)

            def copy_sums(half):
                A.copy(outm[:, half].rearrange("p k f -> p f k"), total[:, :, 1:GP + 1]).then_inc(s["out_copied"], 1)

            A.sem_inc(s["oht_copied"], 2)
            copy_onehots(0)
            with act.Fori(0, NG // U) as i:
                for u in range(U):
                    g, y = i * U + u, u % 2
                    factors(g)
                    copy_parts(g)
                    act.wait_ge(s["zz_done"], g + (CR + 1))
                    A.activation(msg[:, :, D:TW], pairs(zz[:, y, :]), ACT.Exp).then_inc(s["p_done"], 1)
                    act.wait_ge(s["d_done"], g + 1)
                    copy_onehots(g + 1)
                    act.wait_ge(s["msg_done"], g + (CR + 1))
                    A.copy(flat3(parts[:, 0]), flat3(msg[:])).then_inc(s["hi_done"], 1)
                    act.wait_ge(s["scan_done"], g + (CR + 1))
                    act.wait_ge(s_wr[(u + 2) % U], i * 16 + 16)
                    copy_sums(1 - y)
                    A.copy(part[:, :, 0:1], total[:, :, GP:GP + 1])
                    act.wait_ge(s["left_done"], g + 1)
                    A.copy(flat3(parts[:, 1]), flat3(msg[:])).then_inc(s["mid_done"], 1)
            factors(NG)
            copy_parts(NG)
            act.wait_ge(s["scan_done"], NG + CR + 1)
            act.wait_ge(s_wr[(NG + 2) % U], 16 * (NG // U + 1))
            copy_sums((NG + 1) % 2)


def sums_rows(sums, g):
    r = sums.rearrange("(g n k) f -> g n (k f)", n=P, k=GP)
    return r[bass.ds(g, 1)].rearrange("g n f -> (g n) f")


def relation_edges(nc, top, sh, table, sums):
    s = {n: top.sem("r_" + n) for n in ("keep_spread", "keep_copied", "cleared", "oh_done", "part_done", "sum_step",
                                        "sums_done")}
    s_idx = [top.sem(f"r_index_in{u}") for u in range(U)]
    s_got = [top.sem(f"r_rows_in{u}") for u in range(U)]
    s_wr = [top.sem(f"r_written{u}") for u in range(2)]
    with ExitStack() as ctx:
        sb = lambda n, sh_, d=F32: ctx.enter_context(nc.sbuf_tensor("r_" + n, sh_, d))
        idx = sb("index", [P, U, GP], I32)
        rows = sb("rows", [P, U, GP, D])
        onehot = sb("onehot", [P, 2, GP * P])
        keep = sb("keep", [P, NP])
        outm = sb("sums_by_pair", [P, 2, GP, D])
        part = ctx.enter_context(nc.psum_tensor("r_part", [P, 2, GP * D], F32))
        spread = ctx.enter_context(nc.psum_tensor("r_spread", [P, 4, 512], F32))
        block = ctx.enter_context(nc.Block())
        V = nc.vector

        @block.gpsimd
        def _(pool):
            with pool.Fori(0, NG // U) as i:
                for u in range(U):
                    pool.wait_ge(s_idx[u], i * 16 + 16)
                    pool.nop(nofuse=True)
                    pool.wait_ge(s["part_done"], i * U + (u + 1))
                    pool.nop(nofuse=True)
                    for k in range(GP):
                        nc.gpsimd.indirect_dma_start(
                            out=rows[:, u, k, :], out_offset=None, in_=table,
                            in_offset=bass.IndirectOffsetOnAxis(ap=idx[:, u, k:k + 1], axis=0)).then_inc(s_got[u], 16)

        @block.sync
        def _(sp):
            sp.wait_ge(s["cleared"], 1)
            for y in range(2):
                sp.dma_start(sums_rows(sums, (NG + 1) * y), outm[:, y].rearrange("p k f -> p (k f)"))\
                  .then_inc(s_wr[y], 16)
            for u in range(U - 1):
                sp.dma_start(idx[:, u, :], sh["rel_dram"][:, u * GP:(u + 1) * GP]).then_inc(s_idx[u], 16)
            with sp.Fori(0, NG // U) as i:
                for u in range(U):
                    g, ahead = i * U + u, (u + U - 1) % U
                    sp.wait_ge(s["part_done"], g + U)
                    sp.dma_start(idx[:, ahead, :],
                                 sh["rel_dram"][:, bass.ds((g + (U - 1)) * GP, GP)]).then_inc(s_idx[ahead], 16)
                    sp.wait_ge(s["sums_done"], g + 1)
                    sp.dma_start(sums_rows(sums, g + 1), outm[:, u % 2].rearrange("p k f -> p (k f)"))\
                      .then_inc(s_wr[u % 2], 16)
            for y in range(2):
                sp.wait_ge(s_wr[y], 16 * (NG // 2 + 1))
            for u in range(U):
                sp.wait_ge(s_idx[u], 16 * (NG // U + (u < U - 1)))

        @block.vector
        def _(dve):
            def one_hot(g, half):
                V.tensor_tensor(onehot[:, half, :].rearrange("p (k n) -> p k n", k=GP),
                                sh["iota_row"][:].unsqueeze(1).to_broadcast([P, GP, P]),
                                sh["dstrel"][:, bass.ds(g * GP, GP)].unsqueeze(2).to_broadcast([P, GP, P]),
                                ALU.is_equal).then_inc(s["oh_done"], 1)

            V.memset(outm[:], 0.0).then_inc(s["cleared"], 1)
            dve.wait_ge(s["keep_spread"], 1)
            V.tensor_copy(keep[:], spread[:].rearrange("p b f -> p (b f)")[:, 0:NP]).then_inc(s["keep_copied"], 1)
            dve.wait_ge(s["keep_copied"], 1)
            one_hot(0, 0)
            with dve.Fori(0, NG // U) as i:
                for u in range(U):
                    g, y = i * U + u, u % 2
                    dve.wait_ge(s["part_done"], g + U)
                    one_hot(g + 1, 1 - y)
                    dve.wait_ge(s["part_done"], g + (U + 1))
                    dve.wait_ge(s_wr[y], i * 32 + 16 * (u // 2 + 1))
                    for k in range(GP):
                        before = outm[:, y, k - 1, :] if k else outm[:, 1 - y, GP - 1, :]
                        c = V.scalar_tensor_tensor(outm[:, y, k, :], before, keep[:, bass.ds(g * GP + k, 1)],
                                                   part[:, y, k * D:(k + 1) * D], ALU.mult, ALU.add)
                        if k < GP - 1:
                            c.then_inc(s["sum_step"], 1)
                            dve.wait_ge(s["sum_step"], g * (GP - 1) + (k + 1))
                    c.then_inc(s["sums_done"], 1)
                    dve.wait_ge(s["sums_done"], g + 1)

        @block.tensor
        def _(pe):
            for c in range(0, NP, 512):
                w = min(512, NP - c)
                mm = pe.matmul(spread[:, c // 512, 0:w], sh["ones"][0:1, :], sh["same_block"][0:1, c:c + w],
                               start=True, stop=True)
            mm.then_inc(s["keep_spread"], 1)
            pe.sem_inc(s["part_done"], U)
            with pe.Fori(0, NG // U) as i:
                for u in range(U):
                    g, y = i * U + u, u % 2
                    pe.wait_ge(s_got[u], i * (16 * GP) + 16 * GP)
                    pe.wait_ge(s["oh_done"], g + 1)
                    for k in range(GP):
                        mm = pe.matmul(part[:, y, k * D:(k + 1) * D], onehot[:, y, k * P:(k + 1) * P],
                                       rows[:, u, k, :], start=True, stop=True)
                    mm.then_inc(s["part_done"], 1)


def last_phase(nc, top, sh, sums, out):
    s = {n: top.sem("o_" + n) for n in ("used", "all_added", "stored")}
    s_idx = [top.sem(f"o_index_in{h}") for h in range(2)]
    s_ac = [top.sem(f"o_sums_in{h}") for h in range(2)]
    res, whole = sh["res"], N // P
    with ExitStack() as ctx:
        li = ctx.enter_context(nc.sbuf_tensor("o_sum_rows", [P, 2, CB], I32))
        ac = ctx.enter_context(nc.sbuf_tensor("o_sums", [P, 2, CB * D], F32))
        block = ctx.enter_context(nc.Block())
        V = nc.vector

        @block.gpsimd
        def _(pool):
            with pool.Fori(0, NCH // 2) as i:
                for h in range(2):
                    pool.wait_ge(s_idx[h], i * 16 + 16)
                    pool.nop(nofuse=True)
                    pool.wait_ge(s["used"], i * 2 + (h + 1))
                    pool.nop(nofuse=True)
                    for b in range(CB):
                        nc.gpsimd.indirect_dma_start(
                            out=ac[:, h, b * D:(b + 1) * D], out_offset=None, in_=sums,
                            in_offset=bass.IndirectOffsetOnAxis(ap=li[:, h, b:b + 1], axis=0)).then_inc(s_ac[h], 16)

        @block.vector
        def _(dve):
            V.sem_inc(s["used"], 2)
            with dve.Fori(0, NCH // 2) as i:
                for h in range(2):
                    dve.wait_ge(s_ac[h], i * (16 * CB) + 16 * CB)
                    rk = res[:, bass.ds((i * 2 + h) * (CB * D), CB * D)]
                    V.tensor_tensor(rk, rk, ac[:, h, :], ALU.add).then_inc(s["used"], 1)

        @block.sync
        def _(sp):
            with sp.Fori(0, NCH // 2) as i:
                for h in range(2):
                    k = i * 2 + h
                    sp.wait_ge(s["used"], k + 1)
                    sp.dma_start(li[:, h, :], sh["last_dram"][:, bass.ds(k * CB, CB)]).then_inc(s_idx[h], 16)
            sp.wait_ge(s["used"], NCH + 2)
            sp.dma_start(out[0:whole * P, :].rearrange("(b n) f -> n b f", n=P),
                         res[:, 0:whole * D].rearrange("p (b f) -> p b f", f=D)).then_inc(s["stored"], 16)
            sp.dma_start(out[whole * P:N, :], res[0:N - whole * P, whole * D:NB * D]).then_inc(s["stored"], 16)
            sp.wait_ge(s["stored"], 32)


def program(nc, inputs, out):
    with ExitStack() as ctx:
        top = Build(nc, ctx)
        sh = {
            "ident": top.sb("ident", [P, P]),
            "iota_row": top.sb("iota_row", [P, P]),
            "part_f": top.sb("part_f", [P, 1]),
            "ones": top.sb("ones", [P, P]),
            "dstrel": top.sb("dstrel", [P, NP + 2 * GP]),
            "pen_first": top.sb("pen_first", [P, NP]),
            "is_last": top.sb("is_last", [P, NP]),
            "same_block": top.sb("same_block", [1, NP]),
            "pen_cont": top.sb("pen_cont", [1, NP]),
            "pen_chain": top.sb("pen_chain", [1, NP]),
            "ident_b": top.sb("ident_b", [P, P], BF16),
            "ones_b": top.sb("ones_b", [1, P], BF16),
            "log_reset": top.sb("log_reset", [1, GP + NP], BF16),
            "block_at": top.sb("block_at", [1, NP + GP], I32),
            "first_rel": top.sb("first_rel", [GP, NG + 2]),
            "bias": top.sb("bias", [P, 3, D]),
            "wx": top.sb("wx", [D, 3, XW]),
            "w4": top.sb("w4", [D, R, D]),
            "pen_dram": top.dram("pen_dram", (NP, P + 1)),
            "src_dram": top.dram("src_dram", (P, NP + U * GP), I32),
            "rel_dram": top.dram("rel_dram", (P, NP + U * GP), I32),
            "last_dram": top.dram("last_dram", (P, NB), I32),
            "spare": top.dram("spare", (P, 2, P)),
        }
        index_phase(nc, top, inputs["src"], inputs["dst"], inputs["edge_type_16"], sh)
        top.end_phase()
        weights_phase(nc, top, inputs, sh)
        top.end_phase()
        sh["res"] = top.sb("res", [P, NB * D])
        with nc.sbuf_tensor("xp", [P, NB * XW], F32) as xp:
            sh["xp"] = xp
            tables = [top.dram(f"table{l}", (NPAD, TW)) for l in range(3)]
            sums = [top.dram(f"sums{l}", ((NG + 3) * P * GP, SW)) for l in range(3)]
            table4 = top.dram("table4", (NPAD * R, D))
            node_phase(nc, top, sh, "first", 0, x=inputs["x"], table=tables[0])
            top.end_phase()
            attention_edges(nc, top, sh, 0, tables[0], sums[0])
            top.end_phase()
            for l in (1, 2):
                node_phase(nc, top, sh, "next", l, sums=sums[l - 1], table=tables[l])
                top.end_phase()
                attention_edges(nc, top, sh, l, tables[l], sums[l])
                top.end_phase()
            node_phase(nc, top, sh, "relations", 3, sums=sums[2], table=table4)
            top.end_phase()
        sums4 = top.dram("sums4", ((NG + 2) * P * GP, D))
        relation_edges(nc, top, sh, table4, sums4)
        top.end_phase()
        last_phase(nc, top, sh, sums4, out)
        top.end_phase()


INS = ["x", "src", "dst", "edge_type_16", "L0_gnn_W1", "L0_gnn_a1_src", "L0_gnn_a1_dst", "L0_gnn_b1",
       "L0_gnn_W2", "L0_gnn_a2_src", "L0_gnn_a2_dst", "L0_gnn_b2", "L0_gnn_W3", "L0_gnn_a3_src",
       "L0_gnn_a3_dst", "L0_gnn_b3", "L1_gnn_weight"]


def kernel(**inputs):
    import numpy as np
    import concourse.bacc as bacc
    from concourse.bass_utils import run_bass_kernel_spmd as run
    nc = bacc.Bacc("TRN2", target_bir_lowering=False, num_devices=1)
    arrays, handles = {}, {}
    for name in INS:
        a = np.ascontiguousarray(inputs[name])
        arrays[f"in_{name}"] = a
        handles[name] = nc.dram_tensor(f"in_{name}", a.shape, mybir.dt.from_np(a.dtype), kind="ExternalInput").ap()
    out = nc.dram_tensor("out_x", (N, D), F32, kind="ExternalOutput").ap()
    program(nc, handles, out)
    r = run(nc, [arrays], core_ids=[0])
    return r.results[0]["out_x"]
```
